# Optimizing a Trainium2 kernel written in Bass

```python
import numpy as np
import jax
import jax.numpy as jnp

def _softmax(x, axis=-1):
    return jax.nn.softmax(x, axis=axis)

def _gelu(x):
    return jax.nn.gelu(x, approximate=True)

def _silu(x):
    return jax.nn.silu(x)

def _sigmoid(x):
    return jax.nn.sigmoid(x)

def _layernorm(x, axis=-1, eps=1e-05):
    m = jnp.mean(x, axis=axis, keepdims=True)
    v = jnp.var(x, axis=axis, keepdims=True)
    return (x - m) / jnp.sqrt(v + eps)

def _scatter_add(tgt, idx, src, axis=0):
    return tgt.at[idx].add(src)

def _segment_sum(src, seg, n):
    return jax.ops.segment_sum(src, seg, n)
kernel_name = 'mk_prb_d1_jaxref_r8_89bb92'

def setup_inputs(seed: int=0):
    np.random.seed(seed)
    _w = jnp.asarray

    def _L0_attn_setup():
        import jax, jax.numpy as jnp
        import numpy as np
        D_MODEL = 128
        NUM_HEADS = 16
        D_K = D_MODEL // NUM_HEADS

        def _attn(x, Wq, bq, Wk, bk, Wv, bv, Wo, bo):
            B, S, _ = x.shape

            def proj(W, b):
                y = jnp.einsum('bsd,ed->bse', x, W) + b
                return y.reshape(B, S, NUM_HEADS, D_K).transpose(0, 2, 1, 3)
            Q = proj(Wq, bq)
            K = proj(Wk, bk)
            V = proj(Wv, bv)
            scale = 1.0 / np.sqrt(D_K).astype(np.float32)
            scores = jnp.einsum('bhqd,bhkd->bhqk', Q, K) * scale
            attn = jax.nn.softmax(scores, axis=1)
            context = jnp.einsum('bhqk,bhkd->bhqd', attn, V)
            context = context.transpose(0, 2, 1, 3).reshape(B, S, D_MODEL)
            return jnp.einsum('bsd,ed->bse', context, Wo) + bo
        key = jax.random.key(seed)
        ks = jax.random.split(key, 9)
        s = 1.0 / np.sqrt(D_MODEL)
        x = jax.random.normal(ks[0], (2, 256, D_MODEL), dtype=jnp.float32)
        mk = lambda k: jax.random.uniform(k, (D_MODEL, D_MODEL), jnp.float32, -s, s)
        mb = lambda k: jax.random.uniform(k, (D_MODEL,), jnp.float32, -s, s)
        return {'x': x, 'Wq': mk(ks[1]), 'bq': mb(ks[2]), 'Wk': mk(ks[3]), 'bk': mb(ks[4]), 'Wv': mk(ks[5]), 'bv': mb(ks[6]), 'Wo': mk(ks[7]), 'bo': mb(ks[8])}
    _L0_attn_in = _L0_attn_setup()

    def _L0_ffn_setup():
        import jax, jax.numpy as jnp
        import numpy as np
        H = 128
        I = 64
        E = 8
        K = 2
        SI = I * 2
        B, S = (2, 128)

        def _mlp(x, gw, uw, dw):
            return jax.nn.silu(x @ gw.T) * (x @ uw.T) @ dw.T
        key = jax.random.key(seed)
        ks = jax.random.split(key, 9)
        s = 0.02
        return {'x': jax.random.normal(ks[0], (B, S, H), jnp.float32), 'gate_w': jax.random.normal(ks[1], (E, H), jnp.float32) * s, 'lb_bias': jnp.zeros((E,), jnp.float32), 'expert_gate_w': jax.random.normal(ks[2], (E, I, H), jnp.float32) * s, 'expert_up_w': jax.random.normal(ks[3], (E, I, H), jnp.float32) * s, 'expert_down_w': jax.random.normal(ks[4], (E, H, I), jnp.float32) * s, 'shared_gate_w': jax.random.normal(ks[5], (SI, H), jnp.float32) * s, 'shared_up_w': jax.random.normal(ks[6], (SI, H), jnp.float32) * s, 'shared_down_w': jax.random.normal(ks[7], (H, SI), jnp.float32) * s}
    _L0_ffn_in = _L0_ffn_setup()
    _d = {'L0_attn_x': _L0_attn_in['x'], 'L0_attn_Wq': _L0_attn_in['Wq'], 'L0_attn_bq': _L0_attn_in['bq'], 'L0_attn_Wk': _L0_attn_in['Wk'], 'L0_attn_bk': _L0_attn_in['bk'], 'L0_attn_Wv': _L0_attn_in['Wv'], 'L0_attn_bv': _L0_attn_in['bv'], 'L0_attn_Wo': _L0_attn_in['Wo'], 'L0_attn_bo': _L0_attn_in['bo'], 'L0_ffn_gate_w': _L0_ffn_in['gate_w'], 'L0_ffn_lb_bias': _L0_ffn_in['lb_bias'], 'L0_ffn_expert_gate_w': _L0_ffn_in['expert_gate_w'], 'L0_ffn_expert_up_w': _L0_ffn_in['expert_up_w'], 'L0_ffn_expert_down_w': _L0_ffn_in['expert_down_w'], 'L0_ffn_shared_gate_w': _L0_ffn_in['shared_gate_w'], 'L0_ffn_shared_up_w': _L0_ffn_in['shared_up_w'], 'L0_ffn_shared_down_w': _L0_ffn_in['shared_down_w']}
    _x0 = _d['L0_attn_x']
    _d['L0_attn_x'] = jax.random.normal(jax.random.fold_in(jax.random.key(seed), 1), (1, 2048, 128), dtype=_x0.dtype)
    del _x0
    return _d

def reference(L0_attn_x, L0_attn_Wq, L0_attn_bq, L0_attn_Wk, L0_attn_bk, L0_attn_Wv, L0_attn_bv, L0_attn_Wo, L0_attn_bo, L0_ffn_gate_w, L0_ffn_lb_bias, L0_ffn_expert_gate_w, L0_ffn_expert_up_w, L0_ffn_expert_down_w, L0_ffn_shared_gate_w, L0_ffn_shared_up_w, L0_ffn_shared_down_w):

    def _L0_attn_ref(x, Wq, bq, Wk, bk, Wv, bv, Wo, bo):
        import jax, jax.numpy as jnp
        import numpy as np
        D_MODEL = 128
        NUM_HEADS = 16
        D_K = D_MODEL // NUM_HEADS

        def _attn(x, Wq, bq, Wk, bk, Wv, bv, Wo, bo):
            B, S, _ = x.shape

            def proj(W, b):
                y = jnp.einsum('bsd,ed->bse', x, W) + b
                return y.reshape(B, S, NUM_HEADS, D_K).transpose(0, 2, 1, 3)
            Q = proj(Wq, bq)
            K = proj(Wk, bk)
            V = proj(Wv, bv)
            scale = 1.0 / np.sqrt(D_K).astype(np.float32)
            scores = jnp.einsum('bhqd,bhkd->bhqk', Q, K) * scale
            attn = jax.nn.softmax(scores, axis=1)
            context = jnp.einsum('bhqk,bhkd->bhqd', attn, V)
            context = context.transpose(0, 2, 1, 3).reshape(B, S, D_MODEL)
            return jnp.einsum('bsd,ed->bse', context, Wo) + bo
        return _attn(x, Wq, bq, Wk, bk, Wv, bv, Wo, bo)

    def _L0_ffn_ref(x, gate_w, lb_bias, expert_gate_w, expert_up_w, expert_down_w, shared_gate_w, shared_up_w, shared_down_w):
        import jax, jax.numpy as jnp
        import numpy as np
        H = 128
        I = 64
        E = 8
        K = 2
        SI = I * 2
        B, S = (2, 128)

        def _mlp(x, gw, uw, dw):
            return jax.nn.silu(x @ gw.T) * (x @ uw.T) @ dw.T
        b, s, h = x.shape
        xf = x.reshape(-1, h)
        logits = xf @ gate_w.T + lb_bias
        scores = jax.nn.sigmoid(logits.astype(jnp.float32))
        topw, topi = jax.lax.top_k(scores, K)
        topw = (topw / (topw.sum(-1, keepdims=True) + 1e-08)).astype(x.dtype)
        out = jnp.zeros_like(xf)
        for e in range(E):
            m = topi == e
            sel = m.any(axis=-1)
            cnt = m.sum()
            wmean = (topw * m).sum() / jnp.maximum(cnt, 1).astype(topw.dtype)
            y = _mlp(xf, expert_gate_w[e], expert_up_w[e], expert_down_w[e])
            out = out + jnp.where(sel[:, None], y * wmean, jnp.zeros((), x.dtype))
        out = out.reshape(b, s, h)
        out = out + _mlp(x, shared_gate_w, shared_up_w, shared_down_w)
        return out
    x = L0_attn_x
    xn = _layernorm(x, axis=-1)
    x = x + _L0_attn_ref(xn, L0_attn_Wq, L0_attn_bq, L0_attn_Wk, L0_attn_bk, L0_attn_Wv, L0_attn_bv, L0_attn_Wo, L0_attn_bo) + _L0_ffn_ref(xn, L0_ffn_gate_w, L0_ffn_lb_bias, L0_ffn_expert_gate_w, L0_ffn_expert_up_w, L0_ffn_expert_down_w, L0_ffn_shared_gate_w, L0_ffn_shared_up_w, L0_ffn_shared_down_w)
    return x

_drawn_inputs = setup_inputs


def setup_inputs(seed=0):
    import zlib

    import numpy as np

    out = dict(_drawn_inputs(seed))
    spreads = {'L0_ffn_lb_bias': (0.0, 0.8)}
    factors = {'L0_attn_bo': 4.641,
     'L0_ffn_gate_w': 8.0,
     'L0_ffn_expert_gate_w': 8.0,
     'L0_ffn_expert_up_w': 8.0,
     'L0_ffn_expert_down_w': 8.0,
     'L0_ffn_shared_gate_w': 8.0,
     'L0_ffn_shared_up_w': 8.0,
     'L0_ffn_shared_down_w': 8.0,
     'L0_attn_bq': 2.739}
    for name, (base, spread) in spreads.items():
        noise = np.random.default_rng([zlib.crc32(name.encode()), seed]).standard_normal(out[name].shape)
        drawn = base * np.exp(spread * noise) if base else spread * noise
        out[name] = jnp.asarray(drawn.astype(out[name].dtype))
    for name, factor in factors.items():
        out[name] = (out[name] * factor).astype(out[name].dtype)
    return out
```

```python
from contextlib import ExitStack

import numpy as np

import concourse.bass as bass
from concourse import mybir

ALU = mybir.AluOpType
ACT = mybir.ActivationFunctionType
AX = mybir.AxisListType
F32 = mybir.dt.float32
BF16 = mybir.dt.bfloat16

P = 128
S = 2048
D = 128
H = 16
DK = D // H
PARTS = 3
ROWS = PARTS * PARTS * DK
KT = S // P
QBLK = 512
QS = QBLK // P
NB = S // QBLK
PER_BLOCK = KT * QS
UNITS = NB * PER_BLOCK
BODY = 2 * QS
PAIRS = KT // 2
EBUF = 4
SCALE = float(1.0 / np.sqrt(DK).astype(np.float32))
LN_EPS = 1e-5

E = 8
I = 64
HT = (E * I + D) // P
TOP_EPS = 1e-8
TT = S // P

C_Q, C_K, C_V, C_O = 0, D, 2 * D, 3 * D
C_R = 4 * D
C_G = C_R + E
C_U = C_G + HT * P
C_ALL = C_U + HT * P


def layer_kernel(nc, x_in, w_in, down_in, cols_in, rows_in, out):
    with ExitStack() as ctx:
        def sb(name, shape, dt=F32):
            return ctx.enter_context(nc.sbuf_tensor(name, shape, dt))

        def ps(name, shape):
            return ctx.enter_context(nc.psum_tensor(name, shape, F32))

        def sem(name):
            return ctx.enter_context(nc.semaphore(name))

        ps_a = ps("scores_a", [P, 2, 2, 512])
        ps_b = ps("scores_b", [P, 2, 512])
        ps_z = ps("z_bank", [P, 512])
        ps_c = ps("context_bank", [P, 512])
        bank = [ps_a[:, 0, 0, :], ps_a[:, 0, 1, :], ps_a[:, 1, 0, :], ps_a[:, 1, 1, :],
                ps_b[:, 0, :], ps_b[:, 1, :], ps_z[:, :], ps_c[:, :]]

        k_parts_dram = nc.dram_tensor("k_parts", (KT, PARTS, D, P), BF16, kind="Internal").ap()
        q_parts_dram = nc.dram_tensor("q_parts", (KT, PARTS, D, P), BF16, kind="Internal").ap()

        x_sb = sb("x_sb", [P, TT, D])
        xn = sb("xn", [P, TT, D])
        xnT = sb("xnT", [D, S])
        w_sb = sb("w_sb", [D, C_ALL])
        down_sb = sb("down_sb", [P, HT, D])
        cols_sb = sb("cols_sb", [P, 2])
        rows_sb = sb("rows_sb", [P, 2 * D + E])
        ident = sb("ident", [P, P])
        neg_ident = sb("neg_ident", [P, P], BF16)
        zeros = sb("zeros", [P, P], BF16)
        ones_col = sb("ones_col", [P, 1])
        rank = sb("rank", [P, E])
        stats = sb("stats", [P, TT, 6])
        mv = sb("mv", [P, TT, 2])
        ln_t = sb("ln_t", [P, 6, TT])
        q_parts = sb("q_parts_sb", [P, PARTS, S], BF16)
        k_parts = sb("k_parts_sb", [P, PARTS, S], BF16)
        rt = sb("rt", [P, 12, TT, E])
        rs = sb("rs", [P, 6, TT])
        route_sums = sb("route_sums", [P, 2 * E])
        wm = sb("wm", [E, 4])
        sel_pat = sb("sel_pat", [E, E, I])
        sel_w = sb("sel_w", [E, E * I])
        selT = sb("selT", [E, S])
        xn_flat = xn[:, :, :].rearrange("p t d -> p (t d)")
        silu = xn_flat[:, 0:1024].rearrange("p (b n) -> p b n", b=2)
        gu = xn_flat[:, 1024:2048].rearrange("p (b n) -> p b n", b=2)
        hid = sb("hid", [P, 2, HT, 512])

        v_pad = sb("v_pad", [P, KT, 4, 4, 32])
        v_st = sb("v_st", [P, 2, H, 32])
        k_st = sb("k_st", [ROWS, 2, H, P], BF16)
        q_st = sb("q_st", [ROWS, QS, H, P], BF16)
        copy_a = sb("copy_a", [P, 2, 1024], BF16)
        copy_b = sb("copy_b", [P, 1024], BF16)
        mx_a = sb("mx_a", [P, 512], BF16)
        mx_t = sb("mx_t", [P, 2, 512], BF16)
        mx_h = sb("mx_h", [P, 256], BF16)
        mx = sb("mx", [P, P], BF16)
        ex = sb("ex", [P, EBUF, 2048])
        kf, qf, rest = ex[:, 0, :], ex[:, 1, :], ex[:, 2:4, :]
        pairs = hid[:, 0, 0:4, :].rearrange("p a n -> p (a n)").rearrange(
            "p (b h n) -> p b h n", b=2, n=P)
        ctxT = hid[:, 1, 0, :]
        o_sb = hid[:, 1, 1, :].rearrange("p (t d) -> p t d", d=D)

        s_x = [sem(f"x_loaded{c}") for c in range(4)]
        s_wa = sem("attention_weights_loaded")
        s_wm = sem("mlp_weights_loaded")
        s_rows = sem("rows_loaded")
        s_const = sem("constants_ready")
        s_cst = sem("constants_begun")
        s_vz = sem("v_pad_zeroed")
        s_xbo = sem("x_plus_bo")
        s_dve = sem("dve_step")
        s_std = sem("std_ready")
        s_xn = sem("xn_ready")
        s_xT = sem("xn_transposed")
        s_xnT = sem("xnT_copied")
        s_qk = sem("qk_projected")
        s_qkf = sem("qk_biased")
        s_p0 = sem("part0_ready")
        s_r0 = sem("rest0_ready")
        s_p1 = sem("part1_ready")
        s_p2 = sem("part2_ready")
        s_wk = [sem(f"k_parts_written{c}") for c in range(4)]
        s_wq = [sem(f"q_parts_written{c}") for c in range(4)]
        s_vp = sem("v_projected")
        s_vs = sem("v_scattered")
        s_lg = sem("logits_ready")
        s_lb = sem("biased_logits_ready")
        s_le = sem("logits_exp_ready")
        s_sel = sem("selection_ready")
        s_selT = sem("selection_transposed")
        s_selc = sem("selection_copied")
        s_ws = sem("route_sums_over_tokens")
        s_sw = sem("selector_weighted")
        s_gu = sem("gate_up_mask_ready")
        s_silu = sem("silu_ready")
        s_g2 = sem("gated_up_ready")
        s_h = sem("hidden_ready")
        s_dn = sem("down_ready")
        s_base = sem("base_ready")
        s_k = [sem(f"keys_staged{i}") for i in range(2)]
        s_v = [sem(f"values_staged{i}") for i in range(2)]
        s_q = [sem(f"queries_staged{i}") for i in range(QS)]
        s_sca = sem("scores_a_ready")
        s_scb = sem("scores_b_ready")
        s_cpa = sem("scores_a_copied")
        s_cpb = sem("scores_b_copied")
        s_tree = sem("max_tree_step")
        s_m = sem("max_ready")
        s_suba = sem("shifted_a")
        s_subb = sem("shifted_b")
        s_ea = sem("exp_a_ready")
        s_eb = sem("exp_b_ready")
        s_pair = sem("pair_sums_ready")
        s_z = sem("z_ready")
        s_r = sem("reciprocal_ready")
        s_p = sem("probs_ready")
        s_pv = sem("context_added")
        s_ctx = sem("context_copied")
        s_proj = sem("output_projected")
        s_fin = sem("output_ready")
        s_out = sem("output_written")

        TREE = 4

        def wait(eng, s, value):
            if not isinstance(value, int) or value > 0:
                eng.wait_ge(s, value)

        def exists(u, low=0):
            return not isinstance(u, int) or low <= u < UNITS

        def blocks(eng, step, block_start=None):
            def body(qb, pair, first):
                u0 = qb * PER_BLOCK + pair * BODY
                for j in range(BODY):
                    step(u0, j, qb, pair, first)

            body(0, 0, True)
            with eng.Fori(1, PAIRS) as pair:
                body(0, pair, False)
            with eng.Fori(1, NB - 1) as qb:
                body(qb, 0, True)
                with eng.Fori(1, PAIRS) as pair:
                    body(qb, pair, False)
            body(NB - 1, 0, True)
            with eng.Fori(1, PAIRS - 1) as pair:
                body(NB - 1, pair, False)
            body(NB - 1, PAIRS - 1, False)

        block = ctx.enter_context(nc.Block())

        @block.sync
        def _(sp):
            for c in range(4):
                sp.dma_start(x_sb[:, 4 * c:4 * c + 4, :],
                             x_in[512 * c:512 * c + 512, :].rearrange("(t p) d -> p t d", p=P)
                             ).then_inc(s_x[c], 16)
            sp.dma_start(down_sb[:, :, :], down_in).then_inc(s_wm, 16)
            for c in range(4):
                for parts, dram, s, n in ((k_parts, k_parts_dram, s_wk, 2 * c + 1),
                                          (q_parts, q_parts_dram, s_wq, 2 * c + 2)):
                    sp.wait_ge(s_p2, n)
                    for i in range(PARTS):
                        sp.dma_start(
                            dram[4 * c:4 * c + 4, i].rearrange("t r n -> r t n"),
                            parts[:, i, 512 * c:512 * c + 512].rearrange("r (t n) -> r t n", n=P)
                        ).then_inc(s[c], 16)

            def stage_k(kt, i2):
                src = k_parts_dram[bass.ds(kt, 1)].rearrange("a j (d h) n -> (a j d) (h n)", d=DK)
                for i in range(PARTS):
                    sp.dma_start(k_st[24 * i:24 * i + 24, i2].rearrange("r h n -> r (h n)"), src
                                 ).then_inc(s_k[i2], 16)

            def stage_q(qb, s):
                for i in range(PARTS):
                    src = q_parts_dram[bass.ds(qb * QS + s, 1), i].rearrange(
                        "a (d h) n -> (a d) (h n)", d=DK)
                    for j in range(PARTS):
                        r = DK * (PARTS * i + j)
                        sp.dma_start(q_st[r:r + DK, s].rearrange("r h n -> r (h n)"), src
                                     ).then_inc(s_q[s], 16)

            def stage_v(kt, i2):
                sp.dma_start(v_st[:, i2].rearrange("p h c -> p (h c)"),
                             v_pad[:, bass.ds(kt, 1)].rearrange("p a j i c -> p (a j i c)")
                             ).then_inc(s_v[i2], 16)

            def two_tiles(qb, pair, first):
                for i2 in range(2):
                    kt = 2 * pair + i2
                    u = qb * PER_BLOCK + pair * BODY + i2 * QS
                    wait(sp, s_scb, u - QS)
                    stage_k(kt, i2)
                    if first and i2 == 0:
                        for s in range(QS):
                            wait(sp, s_scb, u - QS + s + 1)
                            stage_q(qb, s)
                    wait(sp, s_pv, u - QS)
                    stage_v(kt, i2)

            def store(qb):
                sp.wait_ge(s_fin, qb + 1)
                dst = out[bass.ds(qb * QBLK, QBLK), :].rearrange("(t p) d -> p t d", p=P)
                sp.dma_start(dst, o_sb[:, :, :]).then_inc(s_out, 16)

            for c in range(4):
                sp.wait_ge(s_wk[c], 16 * PARTS)
                sp.wait_ge(s_wq[c], 16 * PARTS)
            sp.wait_ge(s_vs, 16)
            two_tiles(0, 0, True)
            with sp.Fori(1, PAIRS) as pair:
                two_tiles(0, pair, False)
            with sp.Fori(1, NB) as qb:
                two_tiles(qb, 0, True)
                store(qb - 1)
                with sp.Fori(1, PAIRS) as pair:
                    two_tiles(qb, pair, False)
            store(NB - 1)
            sp.wait_ge(s_out, 16 * NB)

        @block.gpsimd
        def _(pool):
            pool.memset(ident[:, :], 0.0).then_inc(s_cst, 1)
            pool.memset(neg_ident[:, :], 0.0).then_inc(s_cst, 1)
            pool.memset(sel_pat[:, :, :], 0.0).then_inc(s_cst, 1)
            pool.wait_ge(s_cst, 3)
            pool.affine_select(out=ident[:, :], in_=ident[:, :], compare_op=ALU.not_equal, fill=1.0,
                               base=0, pattern=[[-1, P]], channel_multiplier=1).then_inc(s_const, 1)
            pool.affine_select(out=neg_ident[:, :], in_=neg_ident[:, :], compare_op=ALU.not_equal,
                               fill=-1.0, base=0, pattern=[[-1, P]], channel_multiplier=1
                               ).then_inc(s_const, 1)
            pool.affine_select(out=sel_pat[:, :, :], in_=sel_pat[:, :, :], compare_op=ALU.not_equal,
                               fill=1.0, base=0, pattern=[[-1, E], [0, I]], channel_multiplier=1
                               ).then_inc(s_const, 1)
            pool.memset(zeros[:, :], 0.0).then_inc(s_const, 1)
            pool.memset(ones_col[:, :], 1.0).then_inc(s_const, 1)
            for e in range(E):
                pool.memset(rank[:, e:e + 1], float(E - e)).then_inc(s_const, 1)
            pool.memset(v_pad[:, :, :, :, :], 0.0).then_inc(s_vz, 1)
            pool.wait_ge(s_xn, 4)
            pool.wait_ge(s_rows, 16)
            pool.tensor_tensor(x_sb[:, :, :], x_sb[:, :, :],
                               rows_sb[:, D:2 * D].unsqueeze(1).broadcast_to([P, TT, D]), ALU.add
                               ).then_inc(s_xbo, 1)

            def step(u0, j, qb, pair, first):
                u = u0 + j
                e = ex[:, j % EBUF, :]
                pool.wait_ge(s_eb, u + 1)
                wait(pool, s_z, u - 1)
                pool.tensor_tensor(pairs[:, j % 2, 0:4, :].rearrange("p h n -> p (h n)"),
                                   e[:, 1024:1536], e[:, 1536:2048], ALU.add).then_inc(s_pair, 1)
                pool.wait_ge(s_ea, u + 1)
                pool.tensor_tensor(pairs[:, j % 2, 4:8, :].rearrange("p h n -> p (h n)"),
                                   e[:, 0:512], e[:, 512:1024], ALU.add).then_inc(s_pair, 1)

            blocks(pool, step)

        @block.scalar
        def _(act):
            act.dma_start(w_sb[:, 0:C_G], w_in[:, 0:C_G]).then_inc(s_wa, 16)
            act.dma_start(cols_sb[:, :], cols_in).then_inc(s_wa, 16)
            act.dma_start(rows_sb[:, :], rows_in.partition_broadcast(P)).then_inc(s_rows, 16)
            act.dma_start(w_sb[:, C_G:C_ALL], w_in[:, C_G:C_ALL]).then_inc(s_wm, 16)

            act.wait_ge(s_dve, 2 * TT + 1)
            act.activation(ln_t[:, 1, :], ln_t[:, 0, :], ACT.Sqrt).then_inc(s_std, 1)

            for c in range(4):
                act.wait_ge(s_xT, c + 1)
                act.copy(xnT[:, 512 * c:512 * c + 512], bank[c]).then_inc(s_xnT, 1)

            act.wait_ge(s_wa, 32)
            for c in range(4):
                for n, (f, parts, col) in enumerate(((kf, k_parts, 1), (qf, q_parts, 0))):
                    sl = slice(512 * c, 512 * c + 512)
                    act.wait_ge(s_qk, 2 * c + n + 1)
                    act.activation(f[:, sl], bank[4 + n], ACT.Identity, bias=cols_sb[:, col:col + 1]
                                   ).then_inc(s_qkf, 1)
                    act.wait_ge(s_qkf, 2 * c + n + 1)
                    act.copy(parts[:, 0, sl], f[:, sl]).then_inc(s_p0, 1)
                    act.wait_ge(s_r0, 2 * c + n + 1)
                    act.copy(parts[:, 1, sl], rest[:, n, sl]).then_inc(s_p1, 1)

            act.wait_ge(s_lb, 1)
            act.activation(rt[:, 1], rt[:, 0], ACT.Exp, scale=-1.0).then_inc(s_le, 1)
            for c in range(4):
                act.wait_ge(s_selT, c + 1)
                act.copy(selT[:, 512 * c:512 * c + 512], bank[c][0:E]).then_inc(s_selc, 1)
            for n in range(4 * HT):
                act.wait_ge(s_gu, n + 1)
                if n >= 2:
                    act.wait_ge(s_h, n - 1)
                act.activation(silu[:, n % 2, :], bank[n % 2], ACT.Silu).then_inc(s_silu, 1)

            def exp_half(sm, done, psum, e, u):
                act.wait_ge(sm, u + 1)
                act.activation(e, psum, ACT.Exp, scale=SCALE).then_inc(done, 1)

            def copy_b_of(u):
                act.wait_ge(s_scb, u + 1)
                act.copy(copy_b[:, :], ps_b[:, :, :].rearrange("p b n -> p (b n)")).then_inc(s_cpb, 1)

            def copy_a_of(u, par):
                act.wait_ge(s_sca, u + 1)
                act.copy(copy_a[:, par, :], ps_a[:, par].rearrange("p b n -> p (b n)")
                         ).then_inc(s_cpa, 1)

            copy_a_of(0, 0)
            copy_b_of(0)
            copy_a_of(1, 1)

            def context_out(uc, qb):
                act.wait_ge(s_pv, uc + 1)
                act.copy(ctxT[:, :], ps_c[:, :]).then_inc(s_ctx, 1)

            def step(u0, j, qb, pair, first):
                u = u0 + j
                e = ex[:, j % EBUF, :]
                wait(act, s_pv, u - EBUF + 1)
                exp_half(s_subb, s_eb, ps_b[:, :, :].rearrange("p b n -> p (b n)"), e[:, 1024:2048], u)
                exp_half(s_suba, s_ea, ps_a[:, j % 2].rearrange("p b n -> p (b n)"), e[:, 0:1024], u)
                if exists(u + 1):
                    copy_b_of(u + 1)
                if exists(u + 2):
                    copy_a_of(u + 2, j % 2)
                if first and j == 2 and not (isinstance(qb, int) and qb == 0):
                    context_out(u - 3, qb - 1)

            blocks(act, step)
            context_out(UNITS - 1, NB - 1)

        @block.vector
        def _(dve):
            steps = [0]

            def link(ins):
                steps[0] += 1
                ins.then_inc(s_dve, 1)
                dve.wait_ge(s_dve, steps[0])

            def note(ins):
                steps[0] += 1
                ins.then_inc(s_dve, 1)

            for t in range(TT):
                if t % 4 == 0:
                    dve.wait_ge(s_x[t // 4], 16)
                note(dve.bn_stats(stats[:, t, :], x_sb[:, t, :]))
            dve.wait_ge(s_dve, steps[0])
            for t in range(TT):
                note(dve.bn_aggr(mv[:, t, :], stats[:, t, :]))
            dve.wait_ge(s_dve, steps[0])
            link(dve.tensor_scalar(ln_t[:, 0, :], mv[:, :, 1], LN_EPS, None, ALU.add))
            dve.wait_ge(s_std, 1)
            link(dve.reciprocal(ln_t[:, 2, :], ln_t[:, 1, :]))
            link(dve.tensor_tensor(ln_t[:, 3, :], ln_t[:, 0, :], ln_t[:, 2, :], ALU.mult))
            link(dve.tensor_tensor(ln_t[:, 4, :], ln_t[:, 3, :], ln_t[:, 1, :], ALU.add))
            link(dve.reciprocal(ln_t[:, 5, :], ln_t[:, 4, :]))
            link(dve.tensor_scalar(ln_t[:, 2, :], ln_t[:, 5, :], 2.0, None, ALU.mult))
            for t in range(TT):
                ins = dve.tensor_scalar(xn[:, t, :], x_sb[:, t, :], mv[:, t, 0:1], ln_t[:, 2, t:t + 1],
                                        ALU.subtract, ALU.mult)
                if t % 4 == 3:
                    ins.then_inc(s_xn, 1)

            for c in range(4):
                for n, (f, parts) in enumerate(((kf, k_parts), (qf, q_parts))):
                    sl = slice(512 * c, 512 * c + 512)
                    dve.wait_ge(s_p0, 2 * c + n + 1)
                    dve.tensor_tensor(rest[:, n, sl], f[:, sl], parts[:, 0, sl], ALU.subtract
                                      ).then_inc(s_r0, 1)
                    dve.wait_ge(s_r0, 2 * c + n + 1)
                    dve.wait_ge(s_p1, 2 * c + n + 1)
                    dve.tensor_tensor(parts[:, 2, sl], rest[:, n, sl], parts[:, 1, sl], ALU.subtract
                                      ).then_inc(s_p2, 1)

            dve.wait_ge(s_vz, 1)
            dve.wait_ge(s_rows, 16)
            for c in range(4):
                dve.wait_ge(s_vp, c + 1)
                src = bank[6 + c % 2].rearrange("p (t j i d) -> p t j i d", t=4, j=4, i=4)
                bias = rows_sb[:, 0:D].rearrange("p (j i d) -> p j i d", j=4, i=4)
                for i in range(4):
                    dve.tensor_tensor(v_pad[:, 4 * c:4 * c + 4, :, i, DK * i:DK * i + DK],
                                      src[:, :, :, i, :],
                                      bias[:, :, i, :].unsqueeze(1).broadcast_to([P, 4, 4, DK]),
                                      ALU.add).then_inc(s_vs, 1)

            dve.wait_ge(s_lg, 1)
            dve.wait_ge(s_const, 5 + E)
            logits = bank[0][:, 0:TT * E].rearrange("p (t e) -> p t e", e=E)
            dve.tensor_tensor(rt[:, 0], logits,
                              rows_sb[:, 2 * D:2 * D + E].unsqueeze(1).broadcast_to([P, TT, E]),
                              ALU.add).then_inc(s_lb, 1)
            dve.wait_ge(s_le, 1)
            link(dve.tensor_scalar(rt[:, 2], rt[:, 1], 1.0, None, ALU.add))
            link(dve.reciprocal(rt[:, 3], rt[:, 2]))

            rank_b = rank[:, :].unsqueeze(1).broadcast_to([P, TT, E])

            def over_experts(v):
                return v.unsqueeze(2).broadcast_to([P, TT, E])

            def top(scores, best, hot, t0, k0):
                link(dve.tensor_reduce(best, scores, AX.X, ALU.max))
                link(dve.tensor_tensor(rt[:, t0], scores, over_experts(best), ALU.is_ge))
                link(dve.tensor_tensor(rt[:, t0 + 1], rt[:, t0], rank_b, ALU.mult))
                link(dve.tensor_reduce(rs[:, k0], rt[:, t0 + 1], AX.X, ALU.max))
                link(dve.tensor_tensor(hot, rt[:, t0 + 1], over_experts(rs[:, k0]), ALU.is_equal))

            top(rt[:, 3], rs[:, 0], rt[:, 6], 4, 2)
            link(dve.scalar_tensor_tensor(rt[:, 7], rt[:, 6], -4.0, rt[:, 3], ALU.mult, ALU.add))
            top(rt[:, 7], rs[:, 1], rt[:, 10], 8, 3)
            dve.tensor_tensor(rt[:, 11], rt[:, 6], rt[:, 10], ALU.add).then_inc(s_sel, 1)
            link(dve.scalar_tensor_tensor(rs[:, 4], rs[:, 0], TOP_EPS, rs[:, 1], ALU.add, ALU.add))
            link(dve.reciprocal(rs[:, 5], rs[:, 4]))
            link(dve.tensor_tensor(rs[:, 2], rs[:, 0], rs[:, 5], ALU.mult))
            link(dve.tensor_tensor(rs[:, 3], rs[:, 1], rs[:, 5], ALU.mult))
            link(dve.tensor_tensor(rt[:, 4], rt[:, 6], over_experts(rs[:, 2]), ALU.mult))
            link(dve.tensor_tensor(rt[:, 5], rt[:, 10], over_experts(rs[:, 3]), ALU.mult))
            link(dve.tensor_tensor(rt[:, 8], rt[:, 4], rt[:, 5], ALU.add))
            dve.wait_ge(s_sel, 1)
            link(dve.tensor_reduce(route_sums[:, 0:E], rt[:, 8].rearrange("p t e -> p e t"),
                                   AX.X, ALU.add))
            link(dve.tensor_reduce(route_sums[:, E:2 * E], rt[:, 11].rearrange("p t e -> p e t"),
                                   AX.X, ALU.add))
            sums_at = steps[0]
            dve.wait_ge(s_ws, 1)
            link(dve.tensor_scalar(wm[:, 0:1], bank[7][0:E, 1:2], 1.0, None, ALU.max))
            link(dve.reciprocal(wm[:, 1:2], wm[:, 0:1]))
            link(dve.tensor_tensor(wm[:, 2:3], bank[7][0:E, 0:1], wm[:, 1:2], ALU.mult))
            dve.tensor_scalar(sel_w[:, :], sel_pat[:, :, :].rearrange("e b c -> e (b c)"),
                              wm[:, 2:3], None, ALU.mult).then_inc(s_sw, 1)

            dve.wait_ge(s_xbo, 1)
            for c in range(4):
                if c >= 2:
                    dve.wait_ge(s_dn, c - 1)
                for p in range(HT):
                    n = HT * c + p
                    dve.wait_ge(s_silu, n + 1)
                    routed = p < HT - 1
                    dst = gu[:, n % 2, :] if routed else hid[:, c % 2, p, :]
                    ins = dve.tensor_tensor(dst, silu[:, n % 2, :], bank[2 + n % 2], ALU.mult)
                    ins.then_inc(s_g2 if routed else s_h, 1)
                    if routed:
                        dve.wait_ge(s_g2, (HT - 1) * c + p + 1)
                        dve.tensor_tensor(hid[:, c % 2, p, :], gu[:, n % 2, :], bank[4 + n % 2],
                                          ALU.mult).then_inc(s_h, 1)
                if c >= 1:
                    dve.wait_ge(s_dn, c)
                    dve.tensor_tensor(
                        x_sb[:, 4 * (c - 1):4 * c, :].rearrange("p t d -> p (t d)"),
                        x_sb[:, 4 * (c - 1):4 * c, :].rearrange("p t d -> p (t d)"),
                        bank[6 + (c - 1) % 2], ALU.add).then_inc(s_base, 1)
            dve.wait_ge(s_dn, 4)
            dve.tensor_tensor(x_sb[:, 12:16, :].rearrange("p t d -> p (t d)"),
                              x_sb[:, 12:16, :].rearrange("p t d -> p (t d)"),
                              bank[7], ALU.add).then_inc(s_base, 1)

            def maximum(u, par):
                def tree(k, ins):
                    ins.then_inc(s_tree, 1)
                    dve.wait_ge(s_tree, TREE * u + k)

                dve.wait_ge(s_cpa, u + 1)
                dve.tensor_tensor(mx_a[:, :], copy_a[:, par, 0:512], copy_a[:, par, 512:1024], ALU.max
                                  ).then_inc(s_tree, 1)
                dve.wait_ge(s_cpb, u + 1)
                tree(2, dve.tensor_tensor(mx_t[:, 0, :], copy_b[:, 0:512], copy_b[:, 512:1024], ALU.max))
                tree(3, dve.tensor_tensor(mx_t[:, 1, :], mx_t[:, 0, :], mx_a[:, :], ALU.max))
                tree(4, dve.tensor_tensor(mx_h[:, :], mx_t[:, 1, 0:256], mx_t[:, 1, 256:512], ALU.max))
                dve.tensor_tensor(mx[:, :], mx_h[:, 0:128], mx_h[:, 128:256], ALU.max).then_inc(s_m, 1)

            def probabilities(u, j):
                r = ps_z[:, 0:P].unsqueeze(1).broadcast_to([P, 8, P])
                wait(dve, s_r, u + 1)
                for half in (1, 0):
                    e = ex[:, j % EBUF, 1024 * half:1024 * half + 1024].rearrange(
                        "p (h n) -> p h n", n=P)
                    dve.tensor_tensor(e, e, r, ALU.mult).then_inc(s_p, 1)

            def reciprocal(u):
                dve.wait_ge(s_z, u + 1)
                dve.reciprocal(ps_z[:, 0:P], ps_z[:, 0:P]).then_inc(s_r, 1)

            def finish(qb):
                dve.wait_ge(s_proj, qb + 1)
                wait(dve, s_out, 16 * qb)
                rows = x_sb[:, bass.ds(qb * QS, QS), :].rearrange("p t d -> p (t d)")
                dve.tensor_tensor(o_sb[:, :, :].rearrange("p t d -> p (t d)"), rows, ps_z[:, :],
                                  ALU.add).then_inc(s_fin, 1)

            maximum(0, 0)

            def step(u0, j, qb, pair, first):
                u = u0 + j
                if exists(u - 2):
                    probabilities(u - 2, j - 2)
                if first and j == 3 and not (isinstance(qb, int) and qb == 0):
                    finish(qb - 1)
                if exists(u + 1):
                    maximum(u + 1, (j + 1) % 2)
                if exists(u - 1):
                    reciprocal(u - 1)

            blocks(dve, step)
            probabilities(UNITS - 2, UNITS - 2)
            reciprocal(UNITS - 1)
            probabilities(UNITS - 1, UNITS - 1)
            finish(NB - 1)

        @block.tensor
        def _(pe):
            pe.wait_ge(s_const, 1)
            for c in range(4):
                pe.wait_ge(s_xn, c + 1)
                for t in range(4):
                    ins = pe.transpose(bank[c][:, P * t:P * t + P], xn[:, 4 * c + t, :], ident[:, :])
                ins.then_inc(s_xT, 1)
            pe.wait_ge(s_wa, 32)
            for c in range(4):
                pe.wait_ge(s_xnT, c + 1)
                for n, col in enumerate((C_K, C_Q)):
                    if c >= 1:
                        pe.wait_ge(s_qkf, 2 * (c - 1) + n + 1)
                    pe.matmul(bank[4 + n], w_sb[:, col:col + D], xnT[:, 512 * c:512 * c + 512],
                              start=True, stop=True).then_inc(s_qk, 1)
            for c in range(4):
                if c >= 2:
                    pe.wait_ge(s_vs, 4 * (c - 1))
                for t in range(4):
                    ins = pe.matmul(bank[6 + c % 2][:, P * t:P * t + P],
                                    xnT[:, P * (4 * c + t):P * (4 * c + t) + P],
                                    w_sb[:, C_V:C_V + D], start=True, stop=True)
                ins.then_inc(s_vp, 1)
            for t in range(TT):
                ins = pe.matmul(bank[0][:, E * t:E * t + E], xnT[:, P * t:P * t + P],
                                w_sb[:, C_R:C_R + E], start=True, stop=True)
            ins.then_inc(s_lg, 1)
            pe.wait_ge(s_sel, 1)
            for c in range(4):
                for t in range(4):
                    ins = pe.transpose(bank[c][0:E, P * t:P * t + P], rt[:, 11, 4 * c + t, :],
                                       ident[:, :])
                ins.then_inc(s_selT, 1)
            pe.wait_ge(s_dve, 2 * TT + 6 + 2 + 5 + 1 + 5 + 7 + 2)
            pe.wait_ge(s_vs, 16)
            pe.wait_ge(s_const, 5 + E)
            for k in range(2):
                ins = pe.matmul(bank[7][0:E, k:k + 1], route_sums[:, E * k:E * k + E], ones_col[:, :],
                                start=True, stop=True)
            ins.then_inc(s_ws, 1)
            pe.wait_ge(s_wm, 32)
            pe.wait_ge(s_sw, 1)
            pe.wait_ge(s_selc, 4)
            pe.wait_ge(s_qkf, 8)

            def down(c):
                pe.wait_ge(s_h, HT * (c + 1))
                if c >= 2:
                    pe.wait_ge(s_base, c - 1)
                for t in range(4):
                    for p in range(HT):
                        ins = pe.matmul(bank[6 + c % 2][:, P * t:P * t + P],
                                        hid[:, c % 2, p, P * t:P * t + P], down_sb[:, p, :],
                                        start=(p == 0), stop=(p == HT - 1))
                ins.then_inc(s_dn, 1)

            for c in range(4):
                for p in range(HT):
                    n = HT * c + p
                    if n >= 2:
                        pe.wait_ge(s_silu, n - 1)
                        pe.wait_ge(s_h, n - 1)
                    tok = xnT[:, 512 * c:512 * c + 512]
                    if p < HT - 1:
                        pe.matmul(bank[4 + n % 2], sel_w[:, P * p:P * p + P],
                                  selT[:, 512 * c:512 * c + 512], start=True, stop=True)
                    pe.matmul(bank[2 + n % 2], w_sb[:, C_U + P * p:C_U + P * p + P], tok,
                              start=True, stop=True)
                    pe.matmul(bank[n % 2], w_sb[:, C_G + P * p:C_G + P * p + P], tok,
                              start=True, stop=True).then_inc(s_gu, 1)
                if c >= 1:
                    down(c - 1)
            down(3)

            def scores(j, du, half):
                k = j + du
                i2 = (k // QS) % 2
                s = k % QS
                for h in range(8):
                    dst = (ps_b if half else ps_a[:, k % 2])[:, h // 4, P * (h % 4):P * (h % 4) + P]
                    ins = pe.matmul(dst, k_st[:, i2, 8 * half + h, :], q_st[:, s, 8 * half + h, :],
                                    start=(h % 4 == 0), stop=True, skip_group_check=True)
                ins.then_inc(s_scb if half else s_sca, 1)

            def scores_a(u0, j, du, qb, pair):
                k = j + du
                u = u0 + k
                if k % QS == 0:
                    tiles = (u // BODY) + 1 if isinstance(u, int) else \
                        qb * PAIRS + pair + (1 if k >= BODY else 0) + 1
                    pe.wait_ge(s_k[(k // QS) % 2], 16 * PARTS * tiles)
                if isinstance(u, int):
                    if u % PER_BLOCK < QS:
                        pe.wait_ge(s_q[k % QS], 16 * PARTS * PARTS * (u // PER_BLOCK + 1))
                elif k >= BODY:
                    pe.wait_ge(s_q[k % QS], 16 * PARTS * PARTS * (qb + (pair + 1) // PAIRS + 1))
                elif isinstance(pair, int) and k < QS:
                    pe.wait_ge(s_q[k % QS], 16 * PARTS * PARTS * (qb + 1))
                scores(j, du, 0)

            def shift(u, j):
                m = mx[:, :].unsqueeze(1).broadcast_to([P, 4, P])
                pe.wait_ge(s_m, u + 1)
                for tile, s in ((ps_b, s_subb), (ps_a[:, j % 2], s_suba)):
                    for b in range(2):
                        ins = pe.matmul(tile[:, b, :].rearrange("p (h n) -> p h n", n=P),
                                        neg_ident[:, :], m, start=False, stop=True,
                                        skip_group_check=True)
                    ins.then_inc(s, 1)

            def context(u, k, opens, qb, pair):
                pe.wait_ge(s_p, 2 * u + 2)
                if k % QS == 0:
                    if isinstance(u, int):
                        pe.wait_ge(s_v[(k // QS) % 2], 16 * (u // BODY + 1))
                    else:
                        pe.wait_ge(s_v[(k // QS) % 2], 16 * (qb * PAIRS + pair + (-1 if k < 0 else 0) + 1))
                if opens:
                    wait(pe, s_ctx, qb)
                    pe.matmul(ps_c[:, :], zeros[:, :], neg_ident[:, :].unsqueeze(1).broadcast_to(
                        [P, 4, P]), start=True, stop=True, skip_group_check=True)
                s = k % QS
                for i in range(4):
                    for jj in range(4):
                        h = 4 * jj + i
                        ins = pe.matmul(ps_c[32 * jj:32 * jj + 32, P * s:P * s + P],
                                        v_st[:, (k // QS) % 2, h, :],
                                        ex[:, k % EBUF, P * h:P * h + P],
                                        start=False, stop=True, skip_group_check=True)
                ins.then_inc(s_pv, 1)

            def z_sum(u, k):
                pe.wait_ge(s_pair, 2 * u + 2)
                wait(pe, s_p, 2 * u)
                for h in range(8):
                    ins = pe.matmul(ps_z[:, 0:P], ident[:, :], pairs[:, k % 2, h, :],
                                    start=(h == 0), stop=(h == 7))
                ins.then_inc(s_z, 1)

            def project(qb, uz):
                pe.wait_ge(s_ctx, qb + 1)
                pe.wait_ge(s_p, 2 * uz + 2)
                for t in range(QS):
                    ins = pe.matmul(ps_z[:, P * t:P * t + P], ctxT[:, P * t:P * t + P],
                                    w_sb[:, C_O:C_O + D], start=True, stop=True)
                ins.then_inc(s_proj, 1)

            pe.wait_ge(s_base, 4)
            pe.wait_ge(s_h, 4 * HT)
            scores_a(0, 0, 0, 0, 0)
            scores(0, 0, 1)
            scores_a(0, 0, 1, 0, 0)

            def step(u0, j, qb, pair, first):
                u = u0 + j
                later = first and not (isinstance(qb, int) and qb == 0)
                shift(u, j)
                if exists(u - 3):
                    context(u - 3, j - 3, first and j == 3, qb, pair)
                if exists(u + 1):
                    pe.wait_ge(s_eb, u + 1)
                    scores(j, 1, 1)
                if exists(u + 2):
                    pe.wait_ge(s_ea, u + 1)
                    scores_a(u0, j, 2, qb, pair)
                if later and j == 3:
                    project(qb - 1, u - 2)
                    pe.wait_ge(s_fin, qb)
                if exists(u - 1):
                    z_sum(u - 1, j - 1)

            blocks(pe, step)
            context(UNITS - 3, BODY - 3, False, NB - 1, PAIRS - 1)
            z_sum(UNITS - 1, BODY - 1)
            context(UNITS - 2, BODY - 2, False, NB - 1, PAIRS - 1)
            context(UNITS - 1, BODY - 1, False, NB - 1, PAIRS - 1)
            project(NB - 1, UNITS - 1)


def kernel(**inputs):
    import concourse.bacc as bacc
    from concourse.bass_utils import run_bass_kernel_spmd

    a = {n.removeprefix("L0_"): np.asarray(v) for n, v in inputs.items()}

    def by_dim(w):
        return w.reshape(-1, H, DK).swapaxes(1, 2).reshape(-1, D)

    w = np.concatenate([
        by_dim(a["attn_Wq"].T), by_dim(a["attn_Wk"].T), a["attn_Wv"].T, a["attn_Wo"].T,
        a["ffn_gate_w"].T,
        a["ffn_expert_gate_w"].reshape(E * I, D).T, a["ffn_shared_gate_w"].T,
        a["ffn_expert_up_w"].reshape(E * I, D).T, a["ffn_shared_up_w"].T], axis=1)
    down = np.concatenate([a["ffn_expert_down_w"].swapaxes(1, 2).reshape(E * I, D),
                           a["ffn_shared_down_w"].T], axis=0)
    arrays = {
        "x": np.ascontiguousarray(a["attn_x"].reshape(S, D)),
        "w": np.ascontiguousarray(w),
        "down": np.ascontiguousarray(down.reshape(HT, P, D).swapaxes(0, 1)),
        "cols": np.ascontiguousarray(np.concatenate(
            [by_dim(a["attn_bq"]), by_dim(a["attn_bk"])], axis=0).T),
        "rows": np.concatenate([a["attn_bv"], a["attn_bo"], a["ffn_lb_bias"]]),
    }
    nc = bacc.Bacc("TRN2", target_bir_lowering=False, num_devices=1)
    args = [nc.dram_tensor(n, v.shape, mybir.dt.from_np(v.dtype), kind="ExternalInput").ap()
            for n, v in arrays.items()]
    out = nc.dram_tensor("out", (S, D), F32, kind="ExternalOutput").ap()
    layer_kernel(nc, *args, out)
    r = run_bass_kernel_spmd(nc, [arrays], core_ids=[0])
    return r.results[0]["out"].reshape(1, S, D)
```

```python
from contextlib import ExitStack

import numpy as np

import concourse.bass as bass
from concourse import mybir

ALU = mybir.AluOpType
ACT = mybir.ActivationFunctionType
AX = mybir.AxisListType
F32 = mybir.dt.float32
BF16 = mybir.dt.bfloat16

P = 128
S = 2048
D = 128
H = 16
DK = D // H
PARTS = 3
THREE = PARTS * DK
ROWS = PARTS * THREE
K_DMAS, Q_DMAS = 1, PARTS
KT = S // P
QBLK = 512
QS = QBLK // P
NB = S // QBLK
PER_BLOCK = KT * QS
UNITS = NB * PER_BLOCK
BODY = 2 * QS
PAIRS = KT // 2
EBUF = 4
SCALE = float(1.0 / np.sqrt(DK).astype(np.float32))
LN_EPS = 1e-5

E = 8
I = 64
HT = (E * I + D) // P
TOP_EPS = 1e-8
TT = S // P

C_Q, C_K, C_V, C_O = 0, D, 2 * D, 3 * D
C_R = 4 * D
C_G = C_R + E
C_U = C_G + HT * P
C_ALL = C_U + HT * P


def layer_kernel(nc, x_in, w_in, down_in, cols_in, rows_in, out):
    with ExitStack() as ctx:
        def sb(name, shape, dt=F32):
            return ctx.enter_context(nc.sbuf_tensor(name, shape, dt))

        def ps(name, shape):
            return ctx.enter_context(nc.psum_tensor(name, shape, F32))

        def sem(name):
            return ctx.enter_context(nc.semaphore(name))

        ps_a = ps("scores_a", [P, 4, 512])
        ps_b = ps("scores_b", [P, 2, 512])
        ps_r = ps("reciprocals", [P, 512])
        ps_c = ps("context_bank", [P, 512])
        bank = [ps_a[:, i, :] for i in range(4)] + [ps_b[:, i, :] for i in range(2)] + [
            ps_r[:, :], ps_c[:, :]]

        k_parts_dram = nc.dram_tensor("k_parts", (KT, PARTS, D, P), BF16, kind="Internal").ap()
        q_parts_dram = nc.dram_tensor("q_parts", (KT, PARTS, D, P), BF16, kind="Internal").ap()

        x_sb = sb("x_sb", [P, TT, D])
        xn = sb("xn", [P, TT, D])
        xnT = sb("xnT", [D, S])
        w_sb = sb("w_sb", [D, C_ALL])
        down_sb = sb("down_sb", [P, HT, D])
        cols_sb = sb("cols_sb", [P, 2])
        rows_sb = sb("rows_sb", [P, 2 * D + E])
        ident = sb("ident", [P, P])
        neg_ident = sb("neg_ident", [P, P], BF16)
        zeros = sb("zeros", [P, P], BF16)
        ones_col = sb("ones_col", [P, 1])
        rank = sb("rank", [P, E])
        stats = sb("stats", [P, TT, 6])
        mv = sb("mv", [P, TT, 2])
        ln_t = sb("ln_t", [P, 6, TT])
        q_parts = sb("q_parts_sb", [P, PARTS, S], BF16)
        k_parts = sb("k_parts_sb", [P, PARTS, S], BF16)
        rt = sb("rt", [P, 11, TT, E])
        rs = sb("rs", [P, 6, TT])
        sel = sb("sel", [P, TT, E], BF16)
        route_sums = sb("route_sums", [P, 2 * E])
        wm = sb("wm", [E, 4])
        sel_pat = sb("sel_pat", [E, E, I])
        sel_pat_bf = sb("sel_pat_bf", [E, E * I], BF16)
        selT = sb("selT", [E, S], BF16)
        weight_of = sb("weight_of", [P, HT - 1])
        xn_flat = xn[:, :, :].rearrange("p t d -> p (t d)")
        silu = xn_flat[:, 0:1024].rearrange("p (b n) -> p b n", b=2)
        gu = xn_flat[:, 1024:2048].rearrange("p (b n) -> p b n", b=2)
        hid = sb("hid", [P, 2, HT, 512])

        v_pad = sb("v_pad", [P, KT, 4, 4, 32])
        v_st = sb("v_st", [P, 2, H, 32])
        k_st = sb("k_st", [ROWS, 2, H, P], BF16)
        q_st = sb("q_st", [ROWS, QS, H, P], BF16)
        copies = sb("copies", [P, 5, 512], BF16)
        mx_t = sb("mx_t", [P, 3, 512], BF16)
        mx_h = sb("mx_h", [P, 256], BF16)
        mx = sb("mx", [P, P], BF16)
        ln_z = sb("ln_z", [P, 2, P])
        r0 = sb("r0", [P, 2, P])
        ex = sb("ex", [P, EBUF, 2048])
        kf, qf, rest = ex[:, 0, :], ex[:, 1, :], ex[:, 2:4, :]
        sum2 = hid[:, 0, 0:4, :].rearrange("p (b g) n -> p b g n", b=2)
        sum4 = hid[:, 1, 0:2, :]
        ctxT = hid[:, 1, 2, :]
        o_sb = hid[:, 1, 3, :].rearrange("p (t d) -> p t d", d=D)

        s_x = [sem(f"x_loaded{c}") for c in range(4)]
        s_wa = sem("attention_weights_loaded")
        s_wm = sem("mlp_weights_loaded")
        s_rows = sem("rows_loaded")
        s_const = sem("constants_ready")
        s_cst = sem("constants_begun")
        s_vz = sem("v_pad_zeroed")
        s_xbo = sem("x_plus_bo")
        s_dve = sem("dve_step")
        s_std = sem("std_ready")
        s_xn = sem("xn_ready")
        s_xT = sem("xn_transposed")
        s_xnT = sem("xnT_copied")
        s_qk = sem("qk_projected")
        s_qkf = sem("qk_biased")
        s_p0 = sem("part0_ready")
        s_r0 = sem("rest0_ready")
        s_p1 = sem("part1_ready")
        s_p2 = sem("part2_ready")
        s_wk = [sem(f"k_parts_written{c}") for c in range(4)]
        s_wq = [sem(f"q_parts_written{c}") for c in range(4)]
        s_vp = sem("v_projected")
        s_vs = sem("v_scattered")
        s_lg = sem("logits_ready")
        s_lb = sem("biased_logits_ready")
        s_le = sem("logits_exp_ready")
        s_var = sem("variances_ready")
        s_sel = sem("selection_ready")
        s_selT = sem("selection_transposed")
        s_selc = sem("selection_copied")
        s_rs = sem("route_sums_ready")
        s_ws = sem("route_sums_over_tokens")
        s_mw = sem("mean_weights_ready")
        s_wh = sem("weights_per_hidden_row")
        s_gate = sem("gate_ready")
        s_um = sem("up_and_mask_ready")
        s_silu = sem("silu_ready")
        s_g2 = sem("gated_up_ready")
        s_h = sem("hidden_ready")
        s_dn = sem("down_ready")
        s_base = sem("base_ready")
        s_k = [sem(f"keys_staged{i}") for i in range(2)]
        s_v = [sem(f"values_staged{i}") for i in range(2)]
        s_q = [sem(f"queries_staged{i}") for i in range(QS)]
        s_sc = [sem(f"scores_ready{g}") for g in range(4)]
        s_cp = [sem(f"scores_copied{g}") for g in range(4)]
        s_tree = sem("max_tree_step")
        s_m = sem("max_ready")
        s_sub = [sem(f"scores_shifted{g}") for g in range(4)]
        s_e = [sem(f"exp_ready{g}") for g in range(4)]
        s_pair = sem("pair_sums_ready")
        s_quad = sem("quad_sums_ready")
        s_z = sem("z_ready")
        s_ln = sem("ln_z_ready")
        s_rr = sem("rough_reciprocal_ready")
        s_nw = sem("newton_product_ready")
        s_r = sem("reciprocal_ready")
        s_p = sem("probs_ready")
        s_pv = sem("context_added")
        s_ctx = sem("context_copied")
        s_proj = sem("output_projected")
        s_fin = sem("output_ready")
        s_out = sem("output_written")

        CONSTS = 6 + E
        TREE = 4

        def wait(eng, s, value):
            if not isinstance(value, int) or value > 0:
                eng.wait_ge(s, value)

        def bank_of(g, par):
            return 2 * g + par if g < 2 else 2 + g

        def z_bank(par):
            return ps_a[:, 1 - par, :]

        def copy_at(g, par):
            return 2 * g + par if g < 2 else 4

        def qk_bank(c, n):
            return 2 + (2 * c + n) % 6

        def v_bank(c):
            return 4 + c % 4

        def exists(u):
            return not isinstance(u, int) or 0 <= u < UNITS

        def blocks(eng, step, block_start=None):
            def body(qb, pair, first):
                u0 = qb * PER_BLOCK + pair * BODY
                for j in range(BODY):
                    step(u0, j, qb, pair, first)

            body(0, 0, True)
            with eng.Fori(1, PAIRS) as pair:
                body(0, pair, False)
            with eng.Fori(1, NB - 1) as qb:
                body(qb, 0, True)
                with eng.Fori(1, PAIRS) as pair:
                    body(qb, pair, False)
            body(NB - 1, 0, True)
            with eng.Fori(1, PAIRS - 1) as pair:
                body(NB - 1, pair, False)
            body(NB - 1, PAIRS - 1, False)

        block = ctx.enter_context(nc.Block())

        @block.sync
        def _(sp):
            for c in range(4):
                sp.dma_start(x_sb[:, 4 * c:4 * c + 4, :],
                             x_in[512 * c:512 * c + 512, :].rearrange("(t p) d -> p t d", p=P)
                             ).then_inc(s_x[c], 16)
            sp.dma_start(down_sb[:, :, :], down_in).then_inc(s_wm, 16)
            for c in range(4):
                for parts, dram, s, n in ((k_parts, k_parts_dram, s_wk, 2 * c + 1),
                                          (q_parts, q_parts_dram, s_wq, 2 * c + 2)):
                    sp.wait_ge(s_p2, n)
                    for i in range(PARTS):
                        sp.dma_start(
                            dram[4 * c:4 * c + 4, i].rearrange("t r n -> r t n"),
                            parts[:, i, 512 * c:512 * c + 512].rearrange("r (t n) -> r t n", n=P)
                        ).then_inc(s[c], 16)

            def parts_of(dram, tile):
                return dram[bass.ds(tile, 1)].rearrange("a i (d h) n -> (a i d) (h n)", d=DK)

            def stage_k(kt, i2):
                sp.dma_start(k_st[:, i2].rearrange("r h n -> r (h n)"),
                             parts_of(k_parts_dram, kt).unsqueeze(0).broadcast_to(
                                 [PARTS, THREE, H * P])).then_inc(s_k[i2], 16)

            def stage_q(qb, s):
                src = parts_of(q_parts_dram, qb * QS + s)
                for i in range(PARTS):
                    sp.dma_start(q_st[THREE * i:THREE * i + THREE, s].rearrange("r h n -> r (h n)"),
                                 src[DK * i:DK * i + DK].unsqueeze(0).broadcast_to([PARTS, DK, H * P])
                                 ).then_inc(s_q[s], 16)

            def stage_v(kt, i2):
                sp.dma_start(v_st[:, i2].rearrange("p h c -> p (h c)"),
                             v_pad[:, bass.ds(kt, 1)].rearrange("p a j i c -> p (a j i c)")
                             ).then_inc(s_v[i2], 16)

            def two_tiles(qb, pair, first):
                for i2 in range(2):
                    kt = 2 * pair + i2
                    u = qb * PER_BLOCK + pair * BODY + i2 * QS
                    wait(sp, s_sc[3], u - QS)
                    stage_k(kt, i2)
                    if first and i2 == 0:
                        for s in range(QS):
                            wait(sp, s_sc[3], u - QS + s + 1)
                            stage_q(qb, s)
                    wait(sp, s_pv, u - QS)
                    stage_v(kt, i2)

            def store(qb):
                sp.wait_ge(s_fin, qb + 1)
                dst = out[bass.ds(qb * QBLK, QBLK), :].rearrange("(t p) d -> p t d", p=P)
                sp.dma_start(dst, o_sb[:, :, :]).then_inc(s_out, 16)

            for c in range(4):
                sp.wait_ge(s_wk[c], 16 * PARTS)
                sp.wait_ge(s_wq[c], 16 * PARTS)
            sp.wait_ge(s_vs, 16)
            two_tiles(0, 0, True)
            with sp.Fori(1, PAIRS) as pair:
                two_tiles(0, pair, False)
            with sp.Fori(1, NB) as qb:
                two_tiles(qb, 0, True)
                store(qb - 1)
                with sp.Fori(1, PAIRS) as pair:
                    two_tiles(qb, pair, False)
            store(NB - 1)
            sp.wait_ge(s_out, 16 * NB)

        @block.gpsimd
        def _(pool):
            pool.memset(ident[:, :], 0.0).then_inc(s_cst, 1)
            pool.memset(neg_ident[:, :], 0.0).then_inc(s_cst, 1)
            pool.memset(sel_pat[:, :, :], 0.0).then_inc(s_cst, 1)
            pool.memset(sel_pat_bf[:, :], 0.0).then_inc(s_cst, 1)
            pool.wait_ge(s_cst, 4)
            pool.affine_select(out=ident[:, :], in_=ident[:, :], compare_op=ALU.not_equal, fill=1.0,
                               base=0, pattern=[[-1, P]], channel_multiplier=1).then_inc(s_const, 1)
            pool.affine_select(out=neg_ident[:, :], in_=neg_ident[:, :], compare_op=ALU.not_equal,
                               fill=-1.0, base=0, pattern=[[-1, P]], channel_multiplier=1
                               ).then_inc(s_const, 1)
            pool.affine_select(out=sel_pat[:, :, :], in_=sel_pat[:, :, :], compare_op=ALU.not_equal,
                               fill=1.0, base=0, pattern=[[-1, E], [0, I]], channel_multiplier=1
                               ).then_inc(s_const, 1)
            pool.affine_select(out=sel_pat_bf[:, :].rearrange("e (b c) -> e b c", c=I),
                               in_=sel_pat_bf[:, :].rearrange("e (b c) -> e b c", c=I),
                               compare_op=ALU.not_equal, fill=1.0, base=0, pattern=[[-1, E], [0, I]],
                               channel_multiplier=1).then_inc(s_const, 1)
            pool.memset(zeros[:, :], 0.0).then_inc(s_const, 1)
            pool.memset(ones_col[:, :], 1.0).then_inc(s_const, 1)
            for e in range(E):
                pool.memset(rank[:, e:e + 1], float(E - e)).then_inc(s_const, 1)
            pool.memset(v_pad[:, :, :, :, :], 0.0).then_inc(s_vz, 1)
            for c in range(4):
                for n, (f, parts) in enumerate(((kf, k_parts), (qf, q_parts))):
                    sl = slice(512 * c, 512 * c + 512)
                    pool.wait_ge(s_p0, 2 * c + n + 1)
                    pool.tensor_tensor(rest[:, n, sl], f[:, sl], parts[:, 0, sl], ALU.subtract
                                       ).then_inc(s_r0, 1)
            for c in range(4):
                for n, parts in enumerate((k_parts, q_parts)):
                    sl = slice(512 * c, 512 * c + 512)
                    pool.wait_ge(s_r0, 2 * c + n + 1)
                    pool.wait_ge(s_p1, 2 * c + n + 1)
                    pool.tensor_tensor(parts[:, 2, sl], rest[:, n, sl], parts[:, 1, sl], ALU.subtract
                                       ).then_inc(s_p2, 1)
            pool.wait_ge(s_xn, 4)
            pool.wait_ge(s_rows, 16)
            pool.tensor_tensor(x_sb[:, :, :], x_sb[:, :, :],
                               rows_sb[:, D:2 * D].unsqueeze(1).broadcast_to([P, TT, D]), ALU.add
                               ).then_inc(s_xbo, 1)

            def step(u0, j, qb, pair, first):
                u = u0 + j
                e = ex[:, j % EBUF, :]
                pool.wait_ge(s_e[2], u + 1)
                pool.wait_ge(s_e[0], u + 1)
                wait(pool, s_quad, u - 1)
                pool.tensor_tensor(sum2[:, j % 2, 0, :], e[:, 1024:1536], e[:, 0:512], ALU.add
                                   ).then_inc(s_pair, 1)
                pool.wait_ge(s_e[3], u + 1)
                pool.wait_ge(s_e[1], u + 1)
                pool.tensor_tensor(sum2[:, j % 2, 1, :], e[:, 1536:2048], e[:, 512:1024], ALU.add
                                   ).then_inc(s_pair, 1)
                pool.wait_ge(s_pair, 2 * u + 2)
                wait(pool, s_z, u - 1)
                pool.tensor_tensor(sum4[:, j % 2, :], sum2[:, j % 2, 0, :], sum2[:, j % 2, 1, :], ALU.add
                                   ).then_inc(s_quad, 1)

            pool.wait_ge(s_dn, 4)
            blocks(pool, step)

        @block.scalar
        def _(act):
            act.dma_start(w_sb[:, 0:C_G], w_in[:, 0:C_G]).then_inc(s_wa, 16)
            act.dma_start(cols_sb[:, :], cols_in).then_inc(s_wa, 16)
            act.dma_start(rows_sb[:, :], rows_in.partition_broadcast(P)).then_inc(s_rows, 16)
            act.dma_start(w_sb[:, C_G:C_ALL], w_in[:, C_G:C_ALL]).then_inc(s_wm, 16)

            act.wait_ge(s_var, 1)
            act.activation(ln_t[:, 1, :], ln_t[:, 0, :], ACT.Sqrt).then_inc(s_std, 1)

            for c in range(4):
                act.wait_ge(s_xT, c + 1)
                act.copy(xnT[:, 512 * c:512 * c + 512], bank[c]).then_inc(s_xnT, 1)

            act.wait_ge(s_lb, 1)
            act.activation(rt[:, 1], rt[:, 0], ACT.Exp, scale=-1.0).then_inc(s_le, 1)

            act.wait_ge(s_wa, 32)
            for c in range(4):
                for n, (f, parts, col) in enumerate(((kf, k_parts, 1), (qf, q_parts, 0))):
                    sl = slice(512 * c, 512 * c + 512)
                    act.wait_ge(s_qk, 2 * c + n + 1)
                    act.activation(f[:, sl], bank[qk_bank(c, n)], ACT.Identity, bias=cols_sb[:, col:col + 1]
                                   ).then_inc(s_qkf, 1)
                    act.wait_ge(s_qkf, 2 * c + n + 1)
                    act.copy(parts[:, 0, sl], f[:, sl]).then_inc(s_p0, 1)
            for c in range(4):
                act.wait_ge(s_selT, c + 1)
                act.activation(selT[:, 512 * c:512 * c + 512], bank[c][0:E], ACT.Identity, scale=-1.0
                               ).then_inc(s_selc, 1)
            for n in range(4 * HT):
                act.wait_ge(s_gate, n + 1)
                if n >= 2:
                    act.wait_ge(s_h, n - 1)
                act.activation(silu[:, n % 2, :], bank[n % 2], ACT.Silu).then_inc(s_silu, 1)
                if n < 8:
                    c, parts = n // 2, (k_parts, q_parts)[n % 2]
                    sl = slice(512 * c, 512 * c + 512)
                    act.wait_ge(s_r0, n + 1)
                    act.copy(parts[:, 1, sl], rest[:, n % 2, sl]).then_inc(s_p1, 1)

            def exp_of(g, u, j):
                act.wait_ge(s_sub[g], u + 1)
                act.activation(ex[:, j % EBUF, 512 * g:512 * g + 512], bank[bank_of(g, j % 2)],
                               ACT.Exp, scale=SCALE).then_inc(s_e[g], 1)

            def copy_of(g, u, par):
                act.wait_ge(s_sc[g], u + 1)
                act.copy(copies[:, copy_at(g, par), :], bank[bank_of(g, par)]).then_inc(s_cp[g], 1)

            def rough_reciprocal(u, par):
                act.wait_ge(s_z, u + 1)
                wait(act, s_r, u - 1)
                act.activation(ln_z[:, par, :], z_bank(par)[:, 0:P], ACT.Ln).then_inc(s_ln, 1)
                act.wait_ge(s_ln, u + 1)
                act.activation(r0[:, par, :], ln_z[:, par, :], ACT.Exp, scale=-1.0).then_inc(s_rr, 1)

            act.preload_act_table_set("natural_log_exp_and_others")
            for g in (0, 1, 2):
                copy_of(g, 0, 0)
            for g in (0, 1):
                copy_of(g, 1, 1)

            def context_out(uc, qb):
                act.wait_ge(s_pv, uc + 1)
                act.copy(ctxT[:, :], ps_c[:, :]).then_inc(s_ctx, 1)

            def step(u0, j, qb, pair, first):
                u = u0 + j
                wait(act, s_pv, u - EBUF + 1)
                for g in (2, 0, 3):
                    exp_of(g, u, j)
                if exists(u + 1):
                    copy_of(2, u + 1, (j + 1) % 2)
                exp_of(1, u, j)
                if exists(u - 1):
                    rough_reciprocal(u - 1, (j - 1) % 2)
                if exists(u + 2):
                    for g in (1, 0):
                        copy_of(g, u + 2, j % 2)
                if first and j == 2 and not (isinstance(qb, int) and qb == 0):
                    context_out(u - 3, qb - 1)

            blocks(act, step)
            rough_reciprocal(UNITS - 1, 1)
            context_out(UNITS - 1, NB - 1)

        @block.vector
        def _(dve):
            steps = [0]

            def link(ins):
                steps[0] += 1
                ins.then_inc(s_dve, 1)
                dve.wait_ge(s_dve, steps[0])

            def note(ins):
                steps[0] += 1
                ins.then_inc(s_dve, 1)

            for t in range(TT):
                if t % 4 == 0:
                    dve.wait_ge(s_x[t // 4], 16)
                note(dve.bn_stats(stats[:, t, :], x_sb[:, t, :]))
            dve.wait_ge(s_dve, steps[0])
            for t in range(TT):
                note(dve.bn_aggr(mv[:, t, :], stats[:, t, :]))
            dve.wait_ge(s_dve, steps[0])
            dve.tensor_scalar(ln_t[:, 0, :], mv[:, :, 1], LN_EPS, None, ALU.add).then_inc(s_var, 1)
            dve.wait_ge(s_std, 1)
            link(dve.reciprocal(ln_t[:, 2, :], ln_t[:, 1, :]))
            link(dve.tensor_tensor(ln_t[:, 3, :], ln_t[:, 0, :], ln_t[:, 2, :], ALU.mult))
            link(dve.tensor_tensor(ln_t[:, 4, :], ln_t[:, 3, :], ln_t[:, 1, :], ALU.add))
            link(dve.reciprocal(ln_t[:, 5, :], ln_t[:, 4, :]))
            link(dve.tensor_scalar(ln_t[:, 2, :], ln_t[:, 5, :], 2.0, None, ALU.mult))
            for t in range(TT):
                ins = dve.tensor_scalar(xn[:, t, :], x_sb[:, t, :], mv[:, t, 0:1], ln_t[:, 2, t:t + 1],
                                        ALU.subtract, ALU.mult)
                if t % 4 == 3:
                    ins.then_inc(s_xn, 1)

            dve.wait_ge(s_lg, 1)
            dve.wait_ge(s_rows, 16)
            dve.wait_ge(s_const, CONSTS)
            logits = bank[0][:, 0:TT * E].rearrange("p (t e) -> p t e", e=E)
            dve.tensor_tensor(rt[:, 0], logits,
                              rows_sb[:, 2 * D:2 * D + E].unsqueeze(1).broadcast_to([P, TT, E]),
                              ALU.add).then_inc(s_lb, 1)
            dve.wait_ge(s_le, 1)
            link(dve.tensor_scalar(rt[:, 2], rt[:, 1], 1.0, None, ALU.add))
            link(dve.reciprocal(rt[:, 3], rt[:, 2]))

            rank_b = rank[:, :].unsqueeze(1).broadcast_to([P, TT, E])

            def over_experts(v):
                return v.unsqueeze(2).broadcast_to([P, TT, E])

            def top(scores, best, hot, t0, k0):
                link(dve.tensor_reduce(best, scores, AX.X, ALU.max))
                link(dve.tensor_tensor(rt[:, t0], scores, over_experts(best), ALU.is_ge))
                link(dve.tensor_tensor(rt[:, t0 + 1], rt[:, t0], rank_b, ALU.mult))
                link(dve.tensor_reduce(rs[:, k0], rt[:, t0 + 1], AX.X, ALU.max))
                link(dve.tensor_tensor(hot, rt[:, t0 + 1], over_experts(rs[:, k0]), ALU.is_equal))

            top(rt[:, 3], rs[:, 0], rt[:, 6], 4, 2)
            link(dve.scalar_tensor_tensor(rt[:, 7], rt[:, 6], -4.0, rt[:, 3], ALU.mult, ALU.add))
            top(rt[:, 7], rs[:, 1], rt[:, 10], 8, 3)
            dve.tensor_tensor(sel[:, :, :], rt[:, 6], rt[:, 10], ALU.add).then_inc(s_sel, 1)

            dve.wait_ge(s_vz, 1)
            for c in range(4):
                dve.wait_ge(s_vp, c + 1)
                src = bank[v_bank(c)].rearrange("p (t j i d) -> p t j i d", t=4, j=4, i=4)
                bias = rows_sb[:, 0:D].rearrange("p (j i d) -> p j i d", j=4, i=4)
                for i in range(4):
                    dve.tensor_tensor(v_pad[:, 4 * c:4 * c + 4, :, i, DK * i:DK * i + DK],
                                      src[:, :, :, i, :],
                                      bias[:, :, i, :].unsqueeze(1).broadcast_to([P, 4, 4, DK]),
                                      ALU.add).then_inc(s_vs, 1)

            link(dve.scalar_tensor_tensor(rs[:, 4], rs[:, 0], TOP_EPS, rs[:, 1], ALU.add, ALU.add))
            link(dve.reciprocal(rs[:, 5], rs[:, 4]))
            link(dve.tensor_tensor(rs[:, 2], rs[:, 0], rs[:, 5], ALU.mult))
            link(dve.tensor_tensor(rs[:, 3], rs[:, 1], rs[:, 5], ALU.mult))
            link(dve.tensor_tensor(rt[:, 4], rt[:, 6], over_experts(rs[:, 2]), ALU.mult))
            link(dve.tensor_tensor(rt[:, 5], rt[:, 10], over_experts(rs[:, 3]), ALU.mult))
            link(dve.tensor_tensor(rt[:, 8], rt[:, 4], rt[:, 5], ALU.add))
            dve.wait_ge(s_sel, 1)
            dve.tensor_reduce(route_sums[:, 0:E], rt[:, 8].rearrange("p t e -> p e t"),
                              AX.X, ALU.add).then_inc(s_rs, 1)
            dve.tensor_reduce(route_sums[:, E:2 * E], sel[:, :, :].rearrange("p t e -> p e t"),
                              AX.X, ALU.add).then_inc(s_rs, 1)
            dve.wait_ge(s_ws, 1)
            link(dve.tensor_scalar(wm[:, 0:1], bank[7][0:E, 1:2], 1.0, None, ALU.max))
            link(dve.reciprocal(wm[:, 1:2], wm[:, 0:1]))
            dve.tensor_tensor(wm[:, 2:3], bank[7][0:E, 0:1], wm[:, 1:2], ALU.mult).then_inc(s_mw, 1)
            dve.wait_ge(s_wh, 1)
            link(dve.tensor_copy(weight_of[:, :], bank[7][:, 8:8 + HT - 1]))

            for c in range(4):
                if c >= 2:
                    dve.wait_ge(s_dn, c - 1)
                for p in range(HT):
                    n = HT * c + p
                    dve.wait_ge(s_silu, n + 1)
                    dve.wait_ge(s_um, n + 1)
                    routed = p < HT - 1
                    dst = gu[:, n % 2, :] if routed else hid[:, c % 2, p, :]
                    ins = dve.tensor_tensor(dst, silu[:, n % 2, :], bank[2 + n % 2], ALU.mult)
                    ins.then_inc(s_g2 if routed else s_h, 1)
                    if routed:
                        dve.wait_ge(s_g2, (HT - 1) * c + p + 1)
                        dve.scalar_tensor_tensor(hid[:, c % 2, p, :], gu[:, n % 2, :],
                                                 weight_of[:, p:p + 1], bank[4 + n % 2],
                                                 ALU.mult, ALU.mult).then_inc(s_h, 1)
                if c == 1:
                    dve.wait_ge(s_xbo, 1)
                if c >= 1:
                    dve.wait_ge(s_dn, c)
                    dve.tensor_tensor(
                        x_sb[:, 4 * (c - 1):4 * c, :].rearrange("p t d -> p (t d)"),
                        x_sb[:, 4 * (c - 1):4 * c, :].rearrange("p t d -> p (t d)"),
                        bank[6 + (c - 1) % 2], ALU.add).then_inc(s_base, 1)
            def tree(u, k, dst, a, b):
                if k > 1:
                    dve.wait_ge(s_tree, TREE * u + k - 1)
                dve.tensor_tensor(dst, a, b, ALU.max).then_inc(s_tree, 1)

            def max_0_7(u, par):
                dve.wait_ge(s_cp[0], u + 1)
                dve.wait_ge(s_cp[1], u + 1)
                tree(u, 1, mx_t[:, 0, :], copies[:, copy_at(0, par), :], copies[:, copy_at(1, par), :])

            def max_8_11(u):
                dve.wait_ge(s_cp[2], u + 1)
                tree(u, 2, mx_t[:, 1, :], mx_t[:, 0, :], copies[:, copy_at(2, 0), :])

            def max_12_15(u):
                dve.wait_ge(s_sc[3], u + 1)
                tree(u, 3, mx_t[:, 2, :], mx_t[:, 1, :], bank[bank_of(3, 0)])

            def max_half(u):
                tree(u, 4, mx_h[:, :], mx_t[:, 2, 0:256], mx_t[:, 2, 256:512])

            def max_one(u):
                dve.wait_ge(s_tree, TREE * (u + 1))
                dve.tensor_tensor(mx[:, :], mx_h[:, 0:128], mx_h[:, 128:256], ALU.max
                                  ).then_inc(s_m, 1)

            def newton_product(u, par):
                dve.wait_ge(s_rr, u + 1)
                wait(dve, s_r, u)
                dve.scalar_tensor_tensor(ps_r[:, 2 * P:3 * P], z_bank(par)[:, 0:P], -1.0, r0[:, par, :],
                                         ALU.mult, ALU.mult).then_inc(s_nw, 1)

            def reciprocal(u, par):
                dve.wait_ge(s_nw, u + 1)
                wait(dve, s_p, u - 1)
                dve.scalar_tensor_tensor(ps_r[:, P * par:P * par + P], ps_r[:, 2 * P:3 * P], 2.0, r0[:, par, :],
                                         ALU.add, ALU.mult).then_inc(s_r, 1)

            def probabilities(u, j):
                r = ps_r[:, P * (j % 2):P * (j % 2) + P].unsqueeze(1).broadcast_to([P, H, P])
                wait(dve, s_r, u + 1)
                e = ex[:, j % EBUF, :].rearrange("p (h n) -> p h n", n=P)
                dve.tensor_tensor(e, e, r, ALU.mult).then_inc(s_p, 1)

            def finish(qb, par):
                dve.wait_ge(s_proj, qb + 1)
                wait(dve, s_out, 16 * qb)
                rows = x_sb[:, bass.ds(qb * QS, QS), :].rearrange("p t d -> p (t d)")
                dve.tensor_tensor(o_sb[:, :, :].rearrange("p t d -> p (t d)"), rows, z_bank(par),
                                  ALU.add).then_inc(s_fin, 1)

            max_0_7(0, 0)
            max_8_11(0)
            max_12_15(0)
            max_half(0)
            max_one(0)
            dve.wait_ge(s_dn, 4)
            dve.tensor_tensor(x_sb[:, 12:16, :].rearrange("p t d -> p (t d)"),
                              x_sb[:, 12:16, :].rearrange("p t d -> p (t d)"),
                              bank[7], ALU.add).then_inc(s_base, 1)

            def step(u0, j, qb, pair, first):
                u = u0 + j
                if exists(u - 2):
                    probabilities(u - 2, j - 2)
                if first and j == 3 and not (isinstance(qb, int) and qb == 0):
                    finish(qb - 1, 0)
                if exists(u + 1):
                    max_0_7(u + 1, (j + 1) % 2)
                    max_8_11(u + 1)
                    max_12_15(u + 1)
                if exists(u - 1):
                    newton_product(u - 1, (j - 1) % 2)
                if exists(u + 1):
                    max_half(u + 1)
                if exists(u - 1):
                    reciprocal(u - 1, (j - 1) % 2)
                if exists(u + 1):
                    max_one(u + 1)

            blocks(dve, step)
            newton_product(UNITS - 1, 1)
            reciprocal(UNITS - 1, 1)
            for u in (UNITS - 2, UNITS - 1):
                probabilities(u, u)
            finish(NB - 1, 1)

        @block.tensor
        def _(pe):
            pe.wait_ge(s_const, 1)
            for c in range(4):
                pe.wait_ge(s_xn, c + 1)
                for t in range(4):
                    ins = pe.transpose(bank[c][:, P * t:P * t + P], xn[:, 4 * c + t, :], ident[:, :])
                ins.then_inc(s_xT, 1)
            pe.wait_ge(s_wm, 32)
            pe.wait_ge(s_xnT, 4)
            for t in range(TT):
                ins = pe.matmul(bank[0][:, E * t:E * t + E], xnT[:, P * t:P * t + P],
                                w_sb[:, C_R:C_R + E], start=True, stop=True)
            ins.then_inc(s_lg, 1)
            pe.wait_ge(s_wa, 32)
            for c in range(4):
                for n, col in enumerate((C_K, C_Q)):
                    if 2 * c + n >= 6:
                        pe.wait_ge(s_qkf, 2 * c + n - 5)
                    pe.matmul(bank[qk_bank(c, n)], w_sb[:, col:col + D], xnT[:, 512 * c:512 * c + 512],
                              start=True, stop=True).then_inc(s_qk, 1)
            for c in range(4):
                pe.wait_ge(s_qkf, 3 + c)
                for t in range(4):
                    ins = pe.matmul(bank[v_bank(c)][:, P * t:P * t + P],
                                    xnT[:, P * (4 * c + t):P * (4 * c + t) + P],
                                    w_sb[:, C_V:C_V + D], start=True, stop=True)
                ins.then_inc(s_vp, 1)
            pe.wait_ge(s_sel, 1)
            pe.wait_ge(s_qkf, 8)
            for c in range(4):
                for t in range(4):
                    ins = pe.matmul(bank[c][0:E, P * t:P * t + P], sel[:, 4 * c + t, :],
                                    neg_ident[:, :], start=True, stop=True)
                ins.then_inc(s_selT, 1)
            pe.wait_ge(s_rs, 2)
            pe.wait_ge(s_vs, 16)
            pe.wait_ge(s_const, CONSTS)
            for k in range(2):
                ins = pe.matmul(bank[7][0:E, k:k + 1], route_sums[:, E * k:E * k + E], ones_col[:, :],
                                start=True, stop=True)
            ins.then_inc(s_ws, 1)
            pe.wait_ge(s_selc, 4)
            pe.wait_ge(s_qkf, 8)

            def down(c):
                pe.wait_ge(s_h, HT * (c + 1))
                if c >= 2:
                    pe.wait_ge(s_base, c - 1)
                for t in range(4):
                    for p in range(HT):
                        ins = pe.matmul(bank[6 + c % 2][:, P * t:P * t + P],
                                        hid[:, c % 2, p, P * t:P * t + P], down_sb[:, p, :],
                                        start=(p == 0), stop=(p == HT - 1))
                ins.then_inc(s_dn, 1)

            for c in range(4):
                for p in range(HT):
                    n = HT * c + p
                    if n >= 2:
                        pe.wait_ge(s_silu, n - 1)
                    tok = xnT[:, 512 * c:512 * c + 512]
                    pe.matmul(bank[n % 2], w_sb[:, C_G + P * p:C_G + P * p + P], tok,
                              start=True, stop=True).then_inc(s_gate, 1)
                    if n >= 2:
                        pe.wait_ge(s_h, n - 1)
                    if p < HT - 1:
                        pe.matmul(bank[4 + n % 2], sel_pat_bf[:, P * p:P * p + P],
                                  selT[:, 512 * c:512 * c + 512], start=True, stop=True)
                    pe.matmul(bank[2 + n % 2], w_sb[:, C_U + P * p:C_U + P * p + P], tok,
                              start=True, stop=True).then_inc(s_um, 1)
                    if n == 0:
                        pe.wait_ge(s_mw, 1)
                        for i in range(HT - 1):
                            ins = pe.matmul(bank[7][:, 8 + i:9 + i],
                                            sel_pat[:, :, :].rearrange("e b c -> e (b c)")[:, P * i:P * i + P],
                                            wm[:, 2:3], start=True, stop=True)
                        ins.then_inc(s_wh, 1)
                if c >= 1:
                    down(c - 1)

            def scores(k, g):
                dst = bank[bank_of(g, k % 2)]
                for i in range(4):
                    ins = pe.matmul(dst[:, P * i:P * i + P], k_st[:, (k // QS) % 2, 4 * g + i, :],
                                    q_st[:, k % QS, 4 * g + i, :],
                                    start=(i == 0), stop=True, skip_group_check=True)
                ins.then_inc(s_sc[g], 1)

            def scores_a(u0, j, du, qb, pair, g=0):
                k = j + du
                u = u0 + k
                if k % QS == 0:
                    tiles = (u // BODY) + 1 if isinstance(u, int) else \
                        qb * PAIRS + pair + (1 if k >= BODY else 0) + 1
                    pe.wait_ge(s_k[(k // QS) % 2], 16 * K_DMAS * tiles)
                if isinstance(u, int):
                    if u % PER_BLOCK < QS:
                        pe.wait_ge(s_q[k % QS], 16 * Q_DMAS * (u // PER_BLOCK + 1))
                elif k >= BODY:
                    pe.wait_ge(s_q[k % QS], 16 * Q_DMAS * (qb + (pair + 1) // PAIRS + 1))
                elif isinstance(pair, int) and k < QS:
                    pe.wait_ge(s_q[k % QS], 16 * Q_DMAS * (qb + 1))
                scores(k, g)

            def shift(u, j):
                m = mx[:, :].unsqueeze(1).broadcast_to([P, 4, P])
                pe.wait_ge(s_m, u + 1)
                for g in (2, 0, 3, 1):
                    pe.matmul(bank[bank_of(g, j % 2)].rearrange("p (h n) -> p h n", n=P),
                              neg_ident[:, :], m, start=False, stop=True, skip_group_check=True
                              ).then_inc(s_sub[g], 1)

            def context(u, k, opens, qb, pair, part):
                if part == 0:
                    pe.wait_ge(s_p, u + 1)
                if part == 0 and k % QS == 0:
                    if isinstance(u, int):
                        pe.wait_ge(s_v[(k // QS) % 2], 16 * (u // BODY + 1))
                    else:
                        pe.wait_ge(s_v[(k // QS) % 2], 16 * (qb * PAIRS + pair + (-1 if k < 0 else 0) + 1))
                if opens and part == 0 and isinstance(u, int) and u == 0:
                    pe.wait_ge(s_base, 4)
                if opens and part == 0:
                    wait(pe, s_ctx, qb)
                    pe.matmul(ps_c[:, :], zeros[:, :], neg_ident[:, :].unsqueeze(1).broadcast_to(
                        [P, 4, P]), start=True, stop=True, skip_group_check=True)
                s = k % QS
                for i in (2 * part, 2 * part + 1):
                    for jj in range(4):
                        h = 4 * jj + i
                        ins = pe.matmul(ps_c[32 * jj:32 * jj + 32, P * s:P * s + P],
                                        v_st[:, (k // QS) % 2, h, :],
                                        ex[:, k % EBUF, P * h:P * h + P],
                                        start=False, stop=True, skip_group_check=True)
                if part:
                    ins.then_inc(s_pv, 1)

            def z_sum(u, k):
                pe.wait_ge(s_quad, u + 1)
                if exists(u + 1):
                    pe.wait_ge(s_e[0], u + 2)
                for h in range(4):
                    ins = pe.matmul(z_bank(k % 2)[:, 0:P], ident[:, :],
                                    sum4[:, k % 2, P * h:P * h + P], start=(h == 0), stop=(h == 3))
                ins.then_inc(s_z, 1)

            def project(qb, par):
                pe.wait_ge(s_ctx, qb + 1)
                for t in range(QS):
                    ins = pe.matmul(z_bank(par)[:, P * t:P * t + P], ctxT[:, P * t:P * t + P],
                                    w_sb[:, C_O:C_O + D], start=True, stop=True)
                ins.then_inc(s_proj, 1)

            pe.wait_ge(s_h, 4 * HT)
            scores_a(0, 0, 0, 0, 0)
            for g in (1, 2, 3):
                scores(0, g)
            scores_a(0, 0, 1, 0, 0)
            scores(1, 1)
            down(3)

            def step(u0, j, qb, pair, first):
                u = u0 + j
                later = first and not (isinstance(qb, int) and qb == 0)
                shift(u, j)
                if exists(u - 3):
                    context(u - 3, j - 3, first and j == 3, qb, pair, 0)
                if exists(u + 1):
                    pe.wait_ge(s_e[2], u + 1)
                    scores(j + 1, 2)
                if later and j == 3:
                    pe.wait_ge(s_e[0], u + 1)
                    project(qb - 1, 0)
                    pe.wait_ge(s_fin, qb)
                if exists(u - 1):
                    z_sum(u - 1, j - 1)
                if exists(u + 1):
                    pe.wait_ge(s_e[3], u + 1)
                    scores(j + 1, 3)
                if exists(u - 3):
                    context(u - 3, j - 3, first and j == 3, qb, pair, 1)
                if exists(u + 2):
                    pe.wait_ge(s_e[1], u + 1)
                    scores_a(u0, j, 2, qb, pair, 1)
                    pe.wait_ge(s_e[0], u + 1)
                    wait(pe, s_nw, u)
                    scores(j + 2, 0)

            blocks(pe, step)
            z_sum(UNITS - 1, BODY - 1)
            for n in (3, 2, 1):
                for part in range(2):
                    context(UNITS - n, BODY - n, False, NB - 1, PAIRS - 1, part)
            pe.wait_ge(s_nw, UNITS)
            project(NB - 1, 1)


def kernel(**inputs):
    import concourse.bacc as bacc
    from concourse.bass_utils import run_bass_kernel_spmd

    a = {n.removeprefix("L0_"): np.asarray(v) for n, v in inputs.items()}

    def by_dim(w):
        return w.reshape(-1, H, DK).swapaxes(1, 2).reshape(-1, D)

    w = np.concatenate([
        by_dim(a["attn_Wq"].T), by_dim(a["attn_Wk"].T), a["attn_Wv"].T, a["attn_Wo"].T,
        a["ffn_gate_w"].T,
        a["ffn_expert_gate_w"].reshape(E * I, D).T, a["ffn_shared_gate_w"].T,
        a["ffn_expert_up_w"].reshape(E * I, D).T, a["ffn_shared_up_w"].T], axis=1)
    down = np.concatenate([a["ffn_expert_down_w"].swapaxes(1, 2).reshape(E * I, D),
                           a["ffn_shared_down_w"].T], axis=0)
    arrays = {
        "x": np.ascontiguousarray(a["attn_x"].reshape(S, D)),
        "w": np.ascontiguousarray(w),
        "down": np.ascontiguousarray(down.reshape(HT, P, D).swapaxes(0, 1)),
        "cols": np.ascontiguousarray(np.concatenate(
            [by_dim(a["attn_bq"]), by_dim(a["attn_bk"])], axis=0).T),
        "rows": np.concatenate([a["attn_bv"], a["attn_bo"], a["ffn_lb_bias"]]),
    }
    nc = bacc.Bacc("TRN2", target_bir_lowering=False, num_devices=1)
    args = [nc.dram_tensor(n, v.shape, mybir.dt.from_np(v.dtype), kind="ExternalInput").ap()
            for n, v in arrays.items()]
    out = nc.dram_tensor("out", (S, D), F32, kind="ExternalOutput").ap()
    layer_kernel(nc, *args, out)
    r = run_bass_kernel_spmd(nc, [arrays], core_ids=[0])
    return r.results[0]["out"].reshape(1, S, D)
```
